# Optimizing a Trainium2 kernel written in Bass

```python
import numpy as np
import jax
import jax.numpy as jnp

def _softmax(x, axis=-1):
    return jax.nn.softmax(x, axis=axis)

def _gelu(x):
    return jax.nn.gelu(x, approximate=True)

def _silu(x):
    return jax.nn.silu(x)

def _sigmoid(x):
    return jax.nn.sigmoid(x)

def _layernorm(x, axis=-1, eps=1e-05):
    m = jnp.mean(x, axis=axis, keepdims=True)
    v = jnp.var(x, axis=axis, keepdims=True)
    return (x - m) / jnp.sqrt(v + eps)

def _scatter_add(tgt, idx, src, axis=0):
    return tgt.at[idx].add(src)

def _segment_sum(src, seg, n):
    return jax.ops.segment_sum(src, seg, n)
kernel_name = 'mk_adaln_ffn_d1_seqx_r2_61f93a'

def setup_inputs(seed: int=0):
    np.random.seed(seed)
    _w = jnp.asarray

    def _rec_inputs():
        import jax
        import jax.numpy as jnp
        _rk = jax.random.key(seed)
        x = -7.109e-05 + 0.9999 * jax.random.normal(jax.random.fold_in(_rk, 1), (8, 512, 2048), jnp.float32)
        _lenS = 512 - jax.random.randint(jax.random.fold_in(_rk, 7), (8,), 0, max(1, 512 // 4) + 1, jnp.int32)
        _lenS2 = 512 - jax.random.randint(jax.random.fold_in(_rk, 8), (8,), 0, max(1, 512 // 4) + 1, jnp.int32)
        itok_B_4_50 = jax.random.randint(jax.random.fold_in(_rk, 11), (8,), 4, 51, jnp.int32)
        return (x, itok_B_4_50)
    x, itok_B_4_50 = _rec_inputs()

    def _L0_cond_setup():
        import jax, jax.numpy as jnp
        import numpy as np
        RANK = 16
        ALPHA = 16.0
        SCALING = ALPHA / RANK
        key = jax.random.key(seed)
        k1, k2, k3, k4 = jax.random.split(key, 4)
        batch, n_tok, d_in, d_out, n_adapters, rank = (8, 1024, 2048, 2048, 64, RANK)
        x = jax.random.normal(k1, (batch, n_tok, d_in), dtype=jnp.float32)
        A = jax.random.normal(k2, (n_adapters, d_out, rank), dtype=jnp.float32) * 0.02
        B = jax.random.normal(k3, (n_adapters, rank, d_in), dtype=jnp.float32)
        adapter_ids = jax.random.randint(k4, (batch,), 0, n_adapters, dtype=jnp.int32)
        return {'x': x, 'A': A, 'B': B, 'adapter_ids': adapter_ids}
    _L0_cond_all = _L0_cond_setup()
    _L0_cond_in = {k: v for k, v in _L0_cond_all.items() if k in ('A', 'B')}
    del _L0_cond_all

    def _L0_ffn_setup():
        import jax, jax.numpy as jnp
        import numpy as np
        BATCH, TOK, DIM, OUT = (4, 1024, 2048, 2048)
        E, R, TOP_K = (8, 16, 2)
        SCALING = 16.0 / R
        key = jax.random.key(seed)
        ks = jax.random.split(key, 6)
        return {'x': jax.random.normal(ks[0], (BATCH, TOK, DIM), dtype=jnp.float32), 'W_base': jax.random.normal(ks[1], (OUT, DIM), dtype=jnp.float32) / np.sqrt(DIM), 'b_base': jax.random.normal(ks[2], (OUT,), dtype=jnp.float32) * 0.01, 'W_gate': jax.random.normal(ks[3], (E, DIM), dtype=jnp.float32) * 0.01, 'A': jax.random.normal(ks[4], (E, R, DIM), dtype=jnp.float32) / np.sqrt(DIM), 'B': jax.random.normal(ks[5], (OUT, OUT // OUT * R * 0 + R), dtype=jnp.float32)[None].repeat(E, 0) * 0.0 + jax.random.normal(ks[5], (E, OUT, R), dtype=jnp.float32) * 0.02}
    _L0_ffn_all = _L0_ffn_setup()
    _L0_ffn_in = {k: v for k, v in _L0_ffn_all.items() if k in ('W_base', 'b_base', 'W_gate', 'A', 'B')}
    del _L0_ffn_all
    return {'x': x, 'itok_B_4_50': itok_B_4_50, 'L0_cond_A': _L0_cond_in['A'], 'L0_cond_B': _L0_cond_in['B'], 'L0_ffn_W_base': _L0_ffn_in['W_base'], 'L0_ffn_b_base': _L0_ffn_in['b_base'], 'L0_ffn_W_gate': _L0_ffn_in['W_gate'], 'L0_ffn_A': _L0_ffn_in['A'], 'L0_ffn_B': _L0_ffn_in['B']}

def reference(x, itok_B_4_50, L0_cond_A, L0_cond_B, L0_ffn_W_base, L0_ffn_b_base, L0_ffn_W_gate, L0_ffn_A, L0_ffn_B):
    import jax
    import jax.numpy as jnp

    def _L0_cond_ref(x, A, B, adapter_ids):
        import jax, jax.numpy as jnp
        import numpy as np
        RANK = 16
        ALPHA = 16.0
        SCALING = ALPHA / RANK
        B_req = B[adapter_ids]
        A_req = A[adapter_ids]
        Bx = jnp.einsum('bni,bri->bnr', x, B_req)
        out = jnp.einsum('bnr,bor->bno', Bx, A_req)
        return out * SCALING

    def _L0_ffn_ref(x, W_base, b_base, W_gate, A, B):
        import jax, jax.numpy as jnp
        import numpy as np
        BATCH, TOK, DIM, OUT = (4, 1024, 2048, 2048)
        E, R, TOP_K = (8, 16, 2)
        SCALING = 16.0 / R
        result = jnp.einsum('bnd,od->bno', x, W_base) + b_base
        logits = jnp.einsum('bnd,ed->bne', x, W_gate)
        probs = jax.nn.softmax(logits.astype(jnp.float32), axis=-1)
        top_p, top_i = jax.lax.top_k(probs, TOP_K)
        top_p = top_p / jnp.sum(top_p, axis=-1, keepdims=True)
        top_p = top_p.astype(x.dtype)
        route_w = jnp.sum(jax.nn.one_hot(top_i, E, dtype=x.dtype) * top_p[..., None], axis=-2)
        h = jnp.einsum('bnd,erd->bner', x, A)
        hw = h * route_w[..., None]
        delta = jnp.einsum('bner,eor->bno', hw, B)
        return result + delta * SCALING
    x = x + _L0_ffn_ref(_L0_cond_ref(x, L0_cond_A, L0_cond_B, itok_B_4_50), L0_ffn_W_base, L0_ffn_b_base, L0_ffn_W_gate, L0_ffn_A, L0_ffn_B)
    return x

_drawn_inputs = setup_inputs


def setup_inputs(seed=0):
    import zlib

    import numpy as np

    out = dict(_drawn_inputs(seed))
    spreads = {}
    factors = {'L0_ffn_b_base': 8.0}
    for name, (base, spread) in spreads.items():
        noise = np.random.default_rng([zlib.crc32(name.encode()), seed]).standard_normal(out[name].shape)
        drawn = base * np.exp(spread * noise) if base else spread * noise
        out[name] = jnp.asarray(drawn.astype(out[name].dtype))
    for name, factor in factors.items():
        out[name] = (out[name] * factor).astype(out[name].dtype)
    return out
```

```python
from contextlib import ExitStack

import concourse.bass as bass
from concourse import mybir

F32 = mybir.dt.float32
BF16 = mybir.dt.bfloat16
I32 = mybir.dt.int32
ALU = mybir.AluOpType
ACT = mybir.ActivationFunctionType
AX_X = mybir.AxisListType.X

P = 128
BATCH, TOK, DIM = 8, 512, 2048
RANK = 16
EXPERTS = 8
CH = DIM // P
QUARTERS = 4
QW = DIM // QUARTERS
QC = CH // QUARTERS
SLOTS = 4
ROUNDS = BATCH // SLOTS
STRIPS = 4
SUB = TOK // P
OUT_BANKS = 4
PARTS = 3
HOLD = RANK + EXPERTS



def adaln_ffn_kernel(nc, xT, ids, A, B, WT, bias, WgT, AeT, BeT, fold, spread, block8, rank_desc, ident, out):
    with ExitStack() as ctx:
        def sb(name, shape, dt):
            return ctx.enter_context(nc.sbuf_tensor(name, shape, dt))

        def ps(name, shape):
            return ctx.enter_context(nc.psum_tensor(name, shape, F32))

        def sem(name):
            return ctx.enter_context(nc.semaphore(name))

        x_sb = sb("x_sb", [P, SLOTS, CH, TOK], F32)
        w_ring = x_sb[:, SLOTS - 1, :, :].rearrange("p (s c) n -> p s c n", s=QUARTERS)
        aeT_sb = x_sb[:, SLOTS - 2, 0:QC, :].rearrange("p c n -> p (c n)").rearrange(
            "p (c n) -> p c n", c=CH)
        early = x_sb[:, SLOTS - 2, QC:3 * QC, :].rearrange("p c n -> p (c n)")
        a_raw = early[:, 0:DIM].rearrange("p (b c r) -> p b c r", b=BATCH, c=CH)
        own_sb = early[:, DIM:DIM + BATCH * P].rearrange("p (b k r) -> p b k r", b=BATCH, r=RANK)
        a_m1 = sb("a_m1", [P, DIM], F32)
        a_sb = a_m1[:, :].rearrange("p (c b r) -> p c b r", c=CH, b=BATCH)
        a_cols = a_m1[:, :].rearrange("p (c k) -> p c k", c=CH)
        m0_sb = sb("m0_sb", [P, DIM], F32)
        m_sb = [m0_sb, a_m1]
        b_raw = sb("b_raw", [P, SLOTS, CH, RANK], F32)
        b_sb = sb("b_sb", [P, SLOTS, CH, 2, RANK], F32)
        be_sb = sb("be_sb", [P, DIM], F32)
        wg_sb = sb("wg_sb", [P, CH, EXPERTS], F32)
        bias_sb = sb("bias_sb", [P, CH], F32)
        ids_sb = sb("ids_sb", [1, BATCH], I32)
        g_parts = sb("g_parts", [P, PARTS, DIM], BF16)
        g_rest = sb("g_rest", [P, 2, QW], F32)
        g_stack = sb("g_stack", [PARTS * RANK, 2, DIM], BF16)
        lg_sb = sb("lg_sb", [P, HOLD], F32)
        head_sb = sb("head_sb", [P, BATCH, HOLD], F32)
        h_sb = sb("h_sb", [P, BATCH, RANK], F32)
        hd_sb = sb("hd_sb", [P, 2, EXPERTS, RANK], F32)
        fold_sb = sb("fold_sb", [PARTS * RANK, P], BF16)
        block8_sb = sb("block8_sb", [P, EXPERTS, RANK], F32)
        desc_sb = sb("desc_sb", [P, SUB, EXPERTS], F32)
        ident_sb = sb("ident_sb", [P, P], F32)
        bx_sb = sb("bx_sb", [P, TOK], F32)
        hold_sb = sb("hold_sb", [P, SUB, HOLD], F32)
        z_sb = sb("z_sb", [P, SUB, EXPERTS, RANK], F32)
        zt_sb = sb("zt_sb", [P, 2, TOK], F32)
        e_a = sb("e_a", [P, SUB, EXPERTS], F32)
        e_b = sb("e_b", [P, SUB, EXPERTS], F32)
        e_c = sb("e_c", [P, SUB, EXPERTS], F32)
        e_d = sb("e_d", [P, SUB, EXPERTS], F32)
        col = sb("col", [P, 8, SUB], F32)

        out_ps = [ps(f"out_ps{i}", [P, TOK]) for i in range(OUT_BANKS)]
        m_ps = [ps(f"m_ps{i}", [P, QW]) for i in range(2)]
        bx_ps = ps("bx_ps", [P, TOK])
        tok_ps = ps("tok_ps", [P, TOK])
        hold_ps = tok_ps[:, 0:SUB * HOLD].rearrange("p (s h) -> p s h", s=SUB)
        head_ps = tok_ps[:, 0:BATCH * HOLD].rearrange("p (b h) -> p b h", b=BATCH)

        ids_loaded = sem("ids_loaded")
        a_loaded = sem("a_loaded")
        be_loaded = sem("be_loaded")
        ae_loaded = sem("ae_loaded")
        consts_loaded = sem("consts_loaded")
        b_loaded = [sem(f"b_loaded{i}") for i in range(SLOTS)]
        a_packed = sem("a_packed")
        own_ready = sem("own_ready")
        b_ready = sem("b_ready")
        w_loaded = [sem(f"w_loaded{i}") for i in range(QUARTERS)]
        w_used = sem("w_used")
        x_loaded = [sem(f"x_loaded{i}") for i in range(SLOTS)]
        x_stored = [sem(f"x_stored{i}") for i in range(SLOTS)]
        h_done = sem("h_done")
        lg_done = sem("lg_done")
        head_done = sem("head_done")
        ps_read = sem("ps_read")
        g_part1 = sem("g_part1")
        g_part2 = sem("g_part2")
        g_part3 = sem("g_part3")
        g_stacked = [sem(f"g_stacked{i}") for i in range(2)]
        hd_ready = sem("hd_ready")
        bx_done = sem("bx_done")
        bx_ready = sem("bx_ready")
        hold_done = sem("hold_done")
        step = sem("step")
        shifted = sem("shifted")
        exp_ready = sem("exp_ready")
        route_ready = sem("route_ready")
        z_ready = sem("z_ready")
        zt_done = sem("zt_done")
        zt_ready = sem("zt_ready")
        m_done = sem("m_done")
        m_ready = sem("m_ready")
        out_done = sem("out_done")
        out_ready = sem("out_ready")

        N_CONSTS = 7
        block = ctx.enter_context(nc.Block())

        @block.sync
        def _(sp):
            sp.dma_start(ids_sb[:, :], ids).then_inc(ids_loaded, 16)
            sp.wait_ge(ids_loaded, 16)
            which = [sp.value_load(ids_sb[0:1, b:b + 1], min_val=0, max_val=A.shape[0] - 1) for b in range(BATCH)]
            for b in range(BATCH):
                sp.dma_start(a_raw[:, b:b + 1, :, :], A[bass.ds(which[b], 1)].rearrange("a p c r -> p a c r")).then_inc(a_loaded, 16)
            sp.dma_start(aeT_sb, AeT).then_inc(ae_loaded, 16)

            def load_w(q, s):
                sp.dma_start(w_ring[:, s, :, :], WT[q, s]).then_inc(w_loaded[s], 16)

            def load_x(b, s):
                sp.dma_start(b_raw[:, s:s + 1, :, :], B[bass.ds(which[b], 1)].rearrange("a p c r -> p a c r")).then_inc(b_loaded[s], 16)
                for q in range(QUARTERS):
                    sp.dma_start(x_sb[:, s, q * QC:(q + 1) * QC, :], xT[b, q]).then_inc(x_loaded[s], 16)

            for s in range(QUARTERS):
                load_w(0, s)
            with sp.Fori(1, QUARTERS) as q:
                for s in range(QUARTERS):
                    sp.wait_ge(w_used, q * QUARTERS + (s + 1 - QUARTERS))
                    sp.dma_start(w_ring[:, s, :, :], WT[bass.ds(q, 1), s].rearrange("a p c n -> p (a c) n")).then_inc(w_loaded[s], 16)
            sp.dma_start(be_sb[:, :], BeT).then_inc(be_loaded, 16)
            load_x(0, 0)
            load_x(1, 1)
            sp.wait_ge(head_done, 1)
            load_x(2, 2)
            sp.wait_ge(w_used, QUARTERS * QUARTERS)
            load_x(3, 3)

            def store(b, s):
                for q in range(QUARTERS):
                    sp.wait_ge(out_ready, b * CH + (q + 1) * QC)
                    sp.dma_start(out[b, q], x_sb[:, s, q * QC:(q + 1) * QC, :]).then_inc(x_stored[s], 16)

            for s in range(SLOTS):
                store(s, s)
                if s > 0:
                    sp.wait_ge(x_stored[s - 1], 16 * QUARTERS)
                    load_x(SLOTS + s - 1, s - 1)
            sp.wait_ge(x_stored[SLOTS - 1], 16 * QUARTERS)
            load_x(BATCH - 1, SLOTS - 1)
            for s in range(SLOTS):
                store(SLOTS + s, s)
            for s in range(SLOTS):
                sp.wait_ge(x_stored[s], ROUNDS * 16 * QUARTERS)

        @block.gpsimd
        def _(pool):
            def double_b(b):
                pool.wait_ge(b_loaded[b % SLOTS], 16 * (b // SLOTS + 1))
                if b >= SLOTS:
                    pool.wait_ge(bx_done, b - SLOTS + 1)
                pool.tensor_copy(b_sb[:, b % SLOTS, :, :, :],
                                 b_raw[:, b % SLOTS, :, :].unsqueeze(2).to_broadcast([P, CH, 2, RANK])).then_inc(b_ready, 1)

            for b in range(SLOTS):
                double_b(b)
            pool.wait_ge(g_part3, QUARTERS)
            for b in range(BATCH):
                if b >= 2:
                    pool.wait_ge(m_done, (b - 1) * QUARTERS)
                for k in range(PARTS):
                    pool.dma_start(g_stack[k * RANK:(k + 1) * RANK, b % 2, :],
                                   g_parts[b * RANK:(b + 1) * RANK, k, :]).then_inc(g_stacked[b % 2], 16)
                if 3 <= b < 3 + SLOTS:
                    double_b(b - 3 + SLOTS)

        @block.scalar
        def _(act):
            act.dma_start(wg_sb[:, :, :], WgT).then_inc(consts_loaded, 16)
            act.dma_start(bias_sb[:, :], bias).then_inc(consts_loaded, 16)
            act.dma_start(fold_sb[:, :], fold).then_inc(consts_loaded, 16)
            act.dma_start(block8_sb[:, :, :], block8).then_inc(consts_loaded, 16)
            act.dma_start(desc_sb[:, :, :], rank_desc).then_inc(consts_loaded, 16)
            act.dma_start(ident_sb[:, :], ident).then_inc(consts_loaded, 16)
            act.dma_start(lg_sb[:, 0:RANK], spread).then_inc(consts_loaded, 16)
            act.wait_ge(a_loaded, 16 * BATCH)
            act.activation(a_sb[:, :, BATCH // 2:, :], a_raw[:, BATCH // 2:, :, :].rearrange("p b c r -> p c b r"),
                           ACT.Copy).then_inc(a_packed, 1)
            with act.Fori(0, QUARTERS // 2) as h:
                for j in range(2):
                    act.wait_ge(w_used, h * (2 * QUARTERS) + (j + 1) * QUARTERS)
                    act.activation(g_parts[:, 0, bass.ds(h * (2 * QW) + j * QW, QW)], m_ps[j][:, :], ACT.Copy).then_inc(g_part1, 1)
                    act.wait_ge(ps_read, h * 2 + (j + 4))
                    act.activation(g_parts[:, 1, bass.ds(h * (2 * QW) + j * QW, QW)], g_rest[:, j, :], ACT.Copy).then_inc(g_part2, 1)

            def copy_m(g, s, q):
                act.wait_ge(m_done, g * (SLOTS * QUARTERS) + (s * QUARTERS + q + 1))
                if s >= 2:
                    act.wait_ge(out_done, g * (SLOTS * CH) + (s - 1) * CH)
                act.activation(m_sb[s % 2][:, q * QW:(q + 1) * QW], m_ps[q % 2][:, :], ACT.Copy).then_inc(m_ready, 1)

            with act.Fori(0, ROUNDS) as g:
                for s in range(SLOTS):
                    act.wait_ge(bx_done, g * SLOTS + (s + 1))
                    if s >= 1:
                        act.wait_ge(hold_done, g * SLOTS + s)
                    act.activation(bx_sb[:, :], bx_ps[:, :], ACT.Copy).then_inc(bx_ready, 1)
                    copy_m(g, s, 0)
                    act.wait_ge(shifted, g * SLOTS + (s + 1))
                    act.activation(e_b[:, :, :], e_a[:, :, :], ACT.Exp).then_inc(exp_ready, 1)
                    for q in range(1, QUARTERS):
                        copy_m(g, s, q)
                    act.wait_ge(zt_done, g * SLOTS + (s + 1))
                    act.activation(zt_sb[:, s % 2, :], bx_ps[:, :], ACT.Copy).then_inc(zt_ready, 1)
                act.wait_ge(out_done, g * (SLOTS * CH) + SLOTS * CH)

        @block.vector
        def _(dve):
            dve.wait_ge(consts_loaded, 16 * N_CONSTS)
            dve.tensor_copy(own_sb, ident_sb[:, :].rearrange("p (b r) -> p b r", b=BATCH).unsqueeze(2).to_broadcast(
                [P, BATCH, P // RANK, RANK])).then_inc(own_ready, 1)
            dve.wait_ge(a_loaded, 16 * BATCH)
            dve.tensor_copy(a_sb[:, :, 0:BATCH // 2, :],
                            a_raw[:, 0:BATCH // 2, :, :].rearrange("p b c r -> p c b r")).then_inc(a_packed, 1)
            dve.wait_ge(h_done, 1)
            dve.tensor_copy(h_sb[:, :, :].rearrange("p b r -> p (b r)"), bx_ps[:, 0:P]).then_inc(ps_read, 1)
            dve.wait_ge(lg_done, 1)
            dve.tensor_scalar(lg_sb[:, RANK:HOLD], tok_ps[:, 0:EXPERTS], 0.5, None, ALU.mult).then_inc(ps_read, 1)
            dve.wait_ge(head_done, 1)
            dve.tensor_copy(head_sb[:, :, :], head_ps).then_inc(ps_read, 1)
            with dve.Fori(0, QUARTERS // 2) as h:
                for j in range(2):
                    part = bass.ds(h * (2 * QW) + j * QW, QW)
                    dve.wait_ge(g_part1, h * 2 + (j + 1))
                    dve.tensor_tensor(g_rest[:, j, :], m_ps[j][:, :], g_parts[:, 0, part], ALU.subtract).then_inc(ps_read, 1)
                    dve.wait_ge(g_part2, h * 2 + (j + 1))
                    dve.tensor_tensor(g_parts[:, 2, part], g_rest[:, j, :], g_parts[:, 1, part], ALU.subtract).then_inc(g_part3, 1)

            def wide(c):
                return col[:, c, :].unsqueeze(2).to_broadcast([P, SUB, EXPERTS])

            N_STEPS = 20

            def routing(g, s):
                count = [0]

                def then(ins):
                    count[0] += 1
                    ins.then_inc(step, 1)
                    dve.wait_ge(step, g * (SLOTS * N_STEPS) + (s * N_STEPS + count[0]))

                dve.wait_ge(hold_done, g * SLOTS + (s + 1))
                then(dve.tensor_copy(hold_sb[:, :, :], hold_ps))
                logits = hold_sb[:, :, RANK:HOLD]
                then(dve.tensor_reduce(col[:, 0, :], logits, AX_X, ALU.max))
                dve.tensor_tensor(e_a[:, :, :], logits, wide(0), ALU.subtract).then_inc(shifted, 1)
                dve.wait_ge(exp_ready, g * SLOTS + (s + 1))
                then(dve.tensor_reduce(col[:, 1, :], e_b[:, :, :], AX_X, ALU.add))
                then(dve.reciprocal(col[:, 2, :], col[:, 1, :]))
                then(dve.tensor_tensor(e_a[:, :, :], e_b[:, :, :], wide(2), ALU.mult))
                then(dve.tensor_reduce(col[:, 3, :], e_a[:, :, :], AX_X, ALU.max))
                then(dve.tensor_tensor(e_b[:, :, :], e_a[:, :, :], wide(3), ALU.is_equal))
                then(dve.tensor_tensor(e_c[:, :, :], e_b[:, :, :], desc_sb[:, :, :], ALU.mult))
                then(dve.tensor_reduce(col[:, 4, :], e_c[:, :, :], AX_X, ALU.max))
                then(dve.tensor_tensor(e_b[:, :, :], e_c[:, :, :], wide(4), ALU.is_equal))
                then(dve.scalar_tensor_tensor(out=e_c[:, :, :], in0=e_b[:, :, :], scalar=-2.0, in1=e_a[:, :, :],
                                              op0=ALU.mult, op1=ALU.add))
                then(dve.tensor_reduce(col[:, 5, :], e_c[:, :, :], AX_X, ALU.max))
                then(dve.tensor_tensor(e_d[:, :, :], e_c[:, :, :], wide(5), ALU.is_equal))
                then(dve.tensor_tensor(e_c[:, :, :], e_d[:, :, :], desc_sb[:, :, :], ALU.mult))
                then(dve.tensor_reduce(col[:, 6, :], e_c[:, :, :], AX_X, ALU.max))
                then(dve.tensor_tensor(e_d[:, :, :], e_c[:, :, :], wide(6), ALU.is_equal))
                then(dve.tensor_tensor(e_c[:, :, :], e_b[:, :, :], e_d[:, :, :], ALU.add))
                then(dve.tensor_tensor(e_d[:, :, :], e_a[:, :, :], e_c[:, :, :], ALU.mult))
                then(dve.tensor_reduce(col[:, 7, :], e_d[:, :, :], AX_X, ALU.add))
                then(dve.reciprocal(col[:, 0, :], col[:, 7, :]))
                assert count[0] == N_STEPS
                dve.tensor_tensor(e_a[:, :, :], e_d[:, :, :], wide(0), ALU.mult).then_inc(route_ready, 1)
                dve.wait_ge(route_ready, g * SLOTS + (s + 1))
                if s >= 1:
                    dve.wait_ge(zt_done, g * SLOTS + s)
                for t in range(SUB):
                    z = dve.tensor_tensor(z_sb[:, t, :, :],
                                          hold_sb[:, t, 0:RANK].unsqueeze(1).to_broadcast([P, EXPERTS, RANK]),
                                          e_a[:, t, :].unsqueeze(2).to_broadcast([P, EXPERTS, RANK]), ALU.mult)
                z.then_inc(z_ready, 1)

            def diagonal(g, s):
                if s >= 2:
                    dve.wait_ge(m_done, g * (SLOTS * QUARTERS) + (s - 1) * QUARTERS)
                b_h = h_sb[:, bass.ds(g * SLOTS + s, 1), :]
                dve.tensor_tensor(hd_sb[:, s % 2, :, :], b_h.to_broadcast([P, EXPERTS, RANK]), block8_sb[:, :, :],
                                  ALU.mult).then_inc(hd_ready, 1)

            def finish(g, s, chunks):
                for c in chunks:
                    dve.wait_ge(out_done, g * (SLOTS * CH) + (s * CH + c + 1))
                    dve.scalar_tensor_tensor(out=x_sb[:, s, c, :], in0=out_ps[c % OUT_BANKS][:, :],
                                             scalar=bias_sb[:, c:c + 1], in1=x_sb[:, s, c, :],
                                             op0=ALU.add, op1=ALU.add).then_inc(out_ready, 1)

            with dve.Fori(0, ROUNDS) as g:
                diagonal(g, 0)
                routing(g, 0)
                for s in range(SLOTS):
                    last = s == SLOTS - 1
                    if not last:
                        diagonal(g, s + 1)
                    finish(g, s, range(0, 8))
                    if not last:
                        routing(g, s + 1)
                    finish(g, s, range(8, CH))

        @block.tensor
        def _(pe):
            pe.wait_ge(a_packed, 2)
            pe.wait_ge(ae_loaded, 16)
            for c in range(CH):
                mm = pe.matmul(bx_ps[:, 0:P], aeT_sb[:, c, :], a_cols[:, c, :], start=(c == 0), stop=(c == CH - 1))
            mm.then_inc(h_done, 1)
            pe.wait_ge(consts_loaded, 16 * N_CONSTS)
            for c in range(CH):
                mm = pe.matmul(tok_ps[:, 0:EXPERTS], a_cols[:, c, :], wg_sb[:, c, :], start=(c == 0), stop=(c == CH - 1))
            mm.then_inc(lg_done, 1)
            pe.wait_ge(own_ready, 1)
            pe.wait_ge(ps_read, 2)
            for b in range(BATCH):
                own = own_sb[:, b, :, :].rearrange("p k r -> p (k r)")
                mm = pe.matmul(head_ps[:, b, :], own, lg_sb[:, :], start=True, stop=True)
            mm.then_inc(head_done, 1)

            with pe.Fori(0, QUARTERS // 2) as h:
                for j in range(2):
                    pe.wait_ge(ps_read, h * 2 + (j + 2))
                    for s in range(QUARTERS):
                        pe.wait_ge(w_loaded[s], h * 32 + 16 * (j + 1))
                        for i in range(QC):
                            c = s * QC + i
                            mm = pe.matmul(m_ps[j][:, :], a_cols[:, c, :], w_ring[:, s, i, :],
                                           start=(c == 0), stop=(c == CH - 1))
                        mm.then_inc(w_used, 1)

            def multiply_b(g, s):
                pe.wait_ge(x_loaded[s], g * (16 * QUARTERS) + 16 * QUARTERS)
                pe.wait_ge(b_ready, g * SLOTS + (s + 1))
                if s >= 1:
                    pe.wait_ge(zt_ready, g * SLOTS + s)
                for c in range(CH):
                    j = c % STRIPS
                    own = b_sb[:, s, c, :, :].rearrange("p k r -> p (k r)")
                    mm = pe.matmul(bx_ps[32 * j:32 * (j + 1), :], own, x_sb[:, s, c, :],
                                   start=(c < STRIPS), stop=(c >= CH - STRIPS))
                mm.then_inc(bx_done, 1)

            def multiply_head(g, s):
                pe.wait_ge(bx_ready, g * SLOTS + (s + 1))
                if s >= 1:
                    pe.wait_ge(z_ready, g * SLOTS + s)
                for t in range(SUB):
                    mm = pe.matmul(hold_ps[:, t, :], bx_sb[:, t * P:(t + 1) * P],
                                   head_sb[:, bass.ds(g * SLOTS + s, 1), :].rearrange("p a h -> p (a h)"),
                                   start=True, stop=True)
                mm.then_inc(hold_done, 1)

            def multiply_m(g, s, quarters):
                for q in quarters:
                    if q == 0:
                        pe.wait_ge(hd_ready, g * SLOTS + (s + 1))
                        pe.wait_ge(g_stacked[s % 2], g * (2 * 16 * PARTS) + (s // 2 + 1) * 16 * PARTS)
                    if s * QUARTERS + q >= 2:
                        pe.wait_ge(m_ready, g * (SLOTS * QUARTERS) + (s * QUARTERS + q - 1))
                    part = slice(q * QW, (q + 1) * QW)
                    pe.matmul(m_ps[q % 2][:, :], hd_sb[:, s % 2, :, :].rearrange("p e r -> p (e r)"), be_sb[:, part],
                              start=True, stop=False)
                    pe.matmul(m_ps[q % 2][:, :], fold_sb[:, :], g_stack[:, s % 2, part],
                              start=False, stop=True).then_inc(m_done, 1)

            def turn_z(g, s):
                pe.wait_ge(z_ready, g * SLOTS + (s + 1))
                for t in range(SUB):
                    mm = pe.transpose(bx_ps[:, t * P:(t + 1) * P], z_sb[:, t, :, :].rearrange("p e r -> p (e r)"),
                                      ident_sb[:, :])
                mm.then_inc(zt_done, 1)

            def multiply_out(g, s, chunks):
                for c in chunks:
                    if c == 0:
                        pe.wait_ge(zt_ready, g * SLOTS + (s + 1))
                    if c % QC == 0:
                        pe.wait_ge(m_ready, g * (SLOTS * QUARTERS) + (s * QUARTERS + c // QC + 1))
                    if s * CH + c >= OUT_BANKS:
                        pe.wait_ge(out_ready, g * (SLOTS * CH) + (s * CH + c + 1 - OUT_BANKS))
                    pe.matmul(out_ps[c % OUT_BANKS][:, :], m_sb[s % 2][:, c * P:(c + 1) * P], zt_sb[:, s % 2, :],
                              start=True, stop=True).then_inc(out_done, 1)

            pe.wait_ge(be_loaded, 16)
            pe.wait_ge(ps_read, 3 + QUARTERS)
            with pe.Fori(0, ROUNDS) as g:
                multiply_b(g, 0)
                multiply_head(g, 0)
                multiply_m(g, 0, range(QUARTERS))
                turn_z(g, 0)
                for s in range(SLOTS):
                    nxt = s + 1 < SLOTS
                    multiply_out(g, s, range(0, 4))
                    if nxt:
                        multiply_b(g, s + 1)
                    multiply_out(g, s, range(4, 8))
                    if nxt:
                        multiply_head(g, s + 1)
                        multiply_m(g, s + 1, range(0, 2))
                    multiply_out(g, s, range(8, 12))
                    if nxt:
                        multiply_m(g, s + 1, range(2, 4))
                        turn_z(g, s + 1)
                    multiply_out(g, s, range(12, 16))
                pe.wait_ge(out_ready, g * (SLOTS * CH) + SLOTS * CH)


def kernel(x, itok_B_4_50, L0_cond_A, L0_cond_B, L0_ffn_W_base, L0_ffn_b_base, L0_ffn_W_gate, L0_ffn_A, L0_ffn_B):
    import ml_dtypes
    import numpy as np
    import concourse.bacc as bacc
    from concourse.bass_utils import run_bass_kernel_spmd

    def lay(a):
        return np.ascontiguousarray(a)

    x, W = np.asarray(x), np.asarray(L0_ffn_W_base)
    eye, rank_eye = np.eye(P, dtype=np.float32), np.eye(RANK, dtype=np.float32)
    arrays = {
        "xT": lay(x.reshape(BATCH, TOK, QUARTERS, QC, P).transpose(0, 2, 4, 3, 1)),
        "ids": lay(np.asarray(itok_B_4_50).reshape(1, BATCH)),
        "A": lay(np.asarray(L0_cond_A).reshape(-1, P, CH, RANK)),
        "B": lay(np.asarray(L0_cond_B).reshape(-1, RANK, CH, P).transpose(0, 3, 2, 1)),
        "WT": lay(W.reshape(QUARTERS, QW, P, QUARTERS, QC).transpose(0, 3, 2, 4, 1)),
        "bias": lay(np.asarray(L0_ffn_b_base).reshape(CH, P).T),
        "WgT": lay(np.asarray(L0_ffn_W_gate).reshape(EXPERTS, P, CH).transpose(1, 2, 0)),
        "AeT": lay(np.asarray(L0_ffn_A).reshape(EXPERTS * RANK, P, CH).transpose(1, 2, 0)),
        "BeT": lay(np.asarray(L0_ffn_B).transpose(0, 2, 1).reshape(EXPERTS * RANK, DIM)),
        "fold": lay(np.tile(rank_eye, (PARTS, EXPERTS)).astype(ml_dtypes.bfloat16)),
        "spread": lay(np.tile(rank_eye * 0.5, (BATCH, 1))),
        "block8": lay(np.kron(np.eye(EXPERTS, dtype=np.float32), np.ones((RANK, RANK), np.float32)).reshape(P, EXPERTS, RANK)),
        "rank_desc": lay(np.broadcast_to(np.arange(EXPERTS, 0, -1, dtype=np.float32), (P, SUB, EXPERTS))),
        "ident": eye,
    }
    nc = bacc.Bacc("TRN2", target_bir_lowering=False, num_devices=1)
    args = [nc.dram_tensor(name, a.shape, mybir.dt.from_np(a.dtype), kind="ExternalInput").ap()
            for name, a in arrays.items()]
    out = nc.dram_tensor("out", (BATCH, QUARTERS, P, QC, TOK), F32, kind="ExternalOutput").ap()
    adaln_ffn_kernel(nc, *args, out)
    r = run_bass_kernel_spmd(nc, [arrays], core_ids=[0])
    got = r.results[0]["out"].reshape(BATCH, QUARTERS, P, QC, TOK)
    return lay(got.transpose(0, 4, 1, 3, 2).reshape(BATCH, TOK, DIM))
```

```python
from contextlib import ExitStack

import concourse.bass as bass
from concourse import mybir

F32 = mybir.dt.float32
BF16 = mybir.dt.bfloat16
I32 = mybir.dt.int32
ALU = mybir.AluOpType
ACT = mybir.ActivationFunctionType
AX_X = mybir.AxisListType.X

P = 128
BATCH, TOK, DIM = 8, 512, 2048
RANK = 16
EXPERTS = 8
CH = DIM // P
QUARTERS = 4
QW = DIM // QUARTERS
QC = CH // QUARTERS
SLOTS = 4
ROUNDS = BATCH // SLOTS
STRIPS = 4
SUB = TOK // P
OUT_BANKS = 4
PARTS = 3
HOLD = RANK + EXPERTS
QUAD = P // 4
A_STEPS = 2
G_STEPS = A_STEPS + QUARTERS



def place(b):
    return 2 * (b % SLOTS) + b // SLOTS


def adaln_ffn_kernel(nc, xT, ids, A, B, WT, bias, WgT, AeT, BeT, fold, spread, block8, rank_desc, ident, out):
    with ExitStack() as ctx:
        def sb(name, shape, dt):
            return ctx.enter_context(nc.sbuf_tensor(name, shape, dt))

        def ps(name, shape):
            return ctx.enter_context(nc.psum_tensor(name, shape, F32))

        def sem(name):
            return ctx.enter_context(nc.semaphore(name))

        x_sb = sb("x_sb", [P, SLOTS, CH, TOK], F32)
        w_ring = x_sb[:, SLOTS - 1, :, :].rearrange("p (s c) n -> p s c n", s=QUARTERS)
        aeT_sb = x_sb[:, SLOTS - 2, 0:QC, :].rearrange("p c n -> p (c n)").rearrange(
            "p (c n) -> p c n", c=CH)
        early = x_sb[:, SLOTS - 2, QC:3 * QC, :].rearrange("p c n -> p (c n)")
        a_raw = early[:, 0:DIM].rearrange("p (b c r) -> p b c r", b=BATCH, c=CH)
        own_sb = early[:, DIM:DIM + BATCH * P].rearrange("p (b k r) -> p b k r", b=BATCH, r=RANK)
        a_m1 = sb("a_m1", [P, DIM], F32)
        a_sb = a_m1[:, :].rearrange("p (c b r) -> p c b r", c=CH, b=BATCH)
        a_cols = a_m1[:, :].rearrange("p (c k) -> p c k", c=CH)
        m0_sb = sb("m0_sb", [P, DIM], F32)
        m_sb = [m0_sb, a_m1]
        b_raw = sb("b_raw", [P, SLOTS, CH, RANK], F32)
        b_sb = sb("b_sb", [P, SLOTS, CH, 2, RANK], F32)
        be_sb = sb("be_sb", [P, DIM], F32)
        wg_sb = sb("wg_sb", [P, CH, EXPERTS], F32)
        bias_sb = sb("bias_sb", [P, CH], F32)
        ids_sb = sb("ids_sb", [1, BATCH], I32)
        g_parts = sb("g_parts", [P, 2, PARTS, QW], BF16)
        g_rest = sb("g_rest", [P, 2, QW], F32)
        g_stack = sb("g_stack", [PARTS * QUAD, SLOTS, DIM], BF16)
        lg_sb = sb("lg_sb", [P, HOLD], F32)
        head_sb = sb("head_sb", [P, BATCH, HOLD], F32)
        h_sb = sb("h_sb", [P, BATCH, RANK], F32)
        hd_sb = sb("hd_sb", [P, 2, EXPERTS, RANK], F32)
        fold_sb = sb("fold_sb", [PARTS * QUAD, ROUNDS, P], BF16)
        fold_cur = sb("fold_cur", [PARTS * QUAD, P], BF16)
        block8_sb = sb("block8_sb", [P, EXPERTS, RANK], F32)
        desc_sb = sb("desc_sb", [P, SUB, EXPERTS], F32)
        ident_sb = sb("ident_sb", [P, P], F32)
        bx_sb = sb("bx_sb", [P, TOK], F32)
        hold_sb = sb("hold_sb", [P, SUB, HOLD], F32)
        z_sb = sb("z_sb", [P, SUB, EXPERTS, RANK], F32)
        zt_sb = sb("zt_sb", [P, 2, TOK], F32)
        e_a = sb("e_a", [P, SUB, EXPERTS], F32)
        e_b = sb("e_b", [P, SUB, EXPERTS], F32)
        e_c = sb("e_c", [P, SUB, EXPERTS], F32)
        e_d = sb("e_d", [P, SUB, EXPERTS], F32)
        col = sb("col", [P, 8, SUB], F32)

        out_ps = [ps(f"out_ps{i}", [P, TOK]) for i in range(OUT_BANKS)]
        m_ps = [ps(f"m_ps{i}", [P, QW]) for i in range(2)]
        bx_ps = ps("bx_ps", [P, TOK])
        tok_ps = ps("tok_ps", [P, TOK])
        hold_ps = tok_ps[:, 0:SUB * HOLD].rearrange("p (s h) -> p s h", s=SUB)
        head_ps = tok_ps[:, 0:BATCH * HOLD].rearrange("p (b h) -> p b h", b=BATCH)

        ids_loaded = sem("ids_loaded")
        a_loaded = sem("a_loaded")
        be_loaded = sem("be_loaded")
        ae_loaded = sem("ae_loaded")
        consts_loaded = sem("consts_loaded")
        ident_loaded = sem("ident_loaded")
        b_loaded = [sem(f"b_loaded{i}") for i in range(SLOTS)]
        a_packed = sem("a_packed")
        own_ready = sem("own_ready")
        b_ready = sem("b_ready")
        w_loaded = [sem(f"w_loaded{i}") for i in range(QUARTERS)]
        w_used = sem("w_used")
        x_loaded = [sem(f"x_loaded{i}") for i in range(SLOTS)]
        x_stored = [sem(f"x_stored{i}") for i in range(SLOTS)]
        h_done = sem("h_done")
        lg_done = sem("lg_done")
        head_done = sem("head_done")
        dve_early = sem("dve_early")
        g_part1 = sem("g_part1")
        g_part2 = sem("g_part2")
        g_part3 = sem("g_part3")
        act_stacked = sem("act_stacked")
        dve_stacked = sem("dve_stacked")
        hd_ready = sem("hd_ready")
        fold_ready = sem("fold_ready")
        bx_done = sem("bx_done")
        bx_ready = sem("bx_ready")
        hold_done = sem("hold_done")
        step = sem("step")
        shifted = sem("shifted")
        exp_ready = sem("exp_ready")
        route_ready = sem("route_ready")
        z_ready = sem("z_ready")
        zt_done = sem("zt_done")
        zt_ready = sem("zt_ready")
        m_done = sem("m_done")
        m_ready = sem("m_ready")
        out_done = sem("out_done")
        out_ready = sem("out_ready")

        N_CONSTS = 6
        block = ctx.enter_context(nc.Block())

        def gather_a(eng, b, index):
            p = place(b)
            eng.dma_start(a_raw[:, p:p + 1, :, :], A[bass.ds(index, 1)].rearrange("a p c r -> p a c r")).then_inc(a_loaded, 16)

        def pack_a(c0, copy):
            return copy(a_sb[:, c0:c0 + QC, :, :], a_raw[:, :, c0:c0 + QC, :].rearrange("p b c r -> p c b r"))

        def stack_g(h, j, k, copy):
            for s in range(SLOTS):
                last = copy(g_stack[k * QUAD:(k + 1) * QUAD, s, bass.ds(h * (2 * QW) + j * QW, QW)],
                            g_parts[s * QUAD:(s + 1) * QUAD, j, k, :])
            return last

        @block.sync
        def _(sp):
            sp.dma_start(ids_sb[:, :], ids).then_inc(ids_loaded, 16)

            def load_w(q, s):
                sp.dma_start(w_ring[:, s, :, :], WT[q, s]).then_inc(w_loaded[s], 16)

            load_w(0, 0)
            sp.wait_ge(ids_loaded, 16)
            which = [None] * BATCH
            for b in range(0, BATCH, 2):
                which[b] = sp.value_load(ids_sb[0:1, b:b + 1], min_val=0, max_val=A.shape[0] - 1)
                gather_a(sp, b, which[b])
            for s in range(1, QUARTERS):
                load_w(0, s)
            for b in range(1, BATCH, 2):
                which[b] = sp.value_load(ids_sb[0:1, b:b + 1], min_val=0, max_val=B.shape[0] - 1)

            def load_b(b, s):
                sp.dma_start(b_raw[:, s:s + 1, :, :], B[bass.ds(which[b], 1)].rearrange("a p c r -> p a c r")).then_inc(b_loaded[s], 16)

            def load_x(b, s, quarters=range(QUARTERS)):
                for q in quarters:
                    sp.dma_start(x_sb[:, s, q * QC:(q + 1) * QC, :], xT[b, q]).then_inc(x_loaded[s], 16)

            load_b(0, 0)
            with sp.Fori(1, QUARTERS) as q:
                for s in range(QUARTERS):
                    sp.wait_ge(w_used, q * QUARTERS + (s + 1 - QUARTERS))
                    sp.dma_start(w_ring[:, s, :, :], WT[bass.ds(q, 1), s].rearrange("a p c n -> p (a c) n")).then_inc(w_loaded[s], 16)
                sp.dma_start(x_sb[:, 0, bass.ds(q * QC - QC, QC), :],
                             xT[0, bass.ds(q - 1, 1)].rearrange("a p c n -> p (a c) n")).then_inc(x_loaded[0], 16)
            sp.dma_start(aeT_sb, AeT).then_inc(ae_loaded, 16)
            load_x(0, 0, [QUARTERS - 1])
            sp.dma_start(be_sb[:, :], BeT).then_inc(be_loaded, 16)
            load_b(1, 1)
            load_x(1, 1)
            sp.wait_ge(w_used, QUARTERS * QUARTERS)
            sp.wait_ge(head_done, 1)
            for s in range(2, SLOTS):
                load_b(s, s)
                load_x(s, s)

            def store(b, s):
                for q in range(QUARTERS):
                    sp.wait_ge(out_ready, b * CH + (q + 1) * QC)
                    sp.dma_start(out[b, q], x_sb[:, s, q * QC:(q + 1) * QC, :]).then_inc(x_stored[s], 16)

            for s in range(SLOTS):
                store(s, s)
                if s > 0:
                    sp.wait_ge(x_stored[s - 1], 16 * QUARTERS)
                    load_b(SLOTS + s - 1, s - 1)
                    load_x(SLOTS + s - 1, s - 1)
            sp.wait_ge(x_stored[SLOTS - 1], 16 * QUARTERS)
            load_b(BATCH - 1, SLOTS - 1)
            load_x(BATCH - 1, SLOTS - 1)
            for s in range(SLOTS):
                store(SLOTS + s, s)
            for s in range(SLOTS):
                sp.wait_ge(x_stored[s], ROUNDS * 16 * QUARTERS)

        @block.gpsimd
        def _(pool):
            def double_b(b):
                pool.wait_ge(b_loaded[b % SLOTS], 16 * (b // SLOTS + 1))
                if b >= SLOTS:
                    pool.wait_ge(bx_done, b - SLOTS + 1)
                pool.tensor_copy(b_sb[:, b % SLOTS, :, :, :],
                                 b_raw[:, b % SLOTS, :, :].unsqueeze(2).to_broadcast([P, CH, 2, RANK])).then_inc(b_ready, 1)

            for b in range(BATCH):
                double_b(b)

        @block.scalar
        def _(act):
            act.wait_ge(ids_loaded, 16)
            for b in range(1, BATCH, 2):
                gather_a(act, b, act.value_load(ids_sb[0:1, b:b + 1], min_val=0, max_val=A.shape[0] - 1))
            act.dma_start(ident_sb[:, :], ident).then_inc(ident_loaded, 16)
            act.dma_start(wg_sb[:, :, :], WgT).then_inc(consts_loaded, 16)
            act.dma_start(bias_sb[:, :], bias).then_inc(consts_loaded, 16)
            act.dma_start(fold_sb[:, :, :], fold).then_inc(consts_loaded, 16)
            act.dma_start(block8_sb[:, :, :], block8).then_inc(consts_loaded, 16)
            act.dma_start(desc_sb[:, :, :], rank_desc).then_inc(consts_loaded, 16)
            act.dma_start(lg_sb[:, 0:RANK], spread).then_inc(consts_loaded, 16)
            act.wait_ge(a_loaded, 16 * BATCH)
            for c0 in (QC, 3 * QC):
                pack_a(c0, lambda o, i: act.activation(o, i, ACT.Copy)).then_inc(a_packed, 1)

            with act.Fori(0, QUARTERS // 2) as h:
                for j in range(2):
                    act.wait_ge(w_used, h * (2 * QUARTERS) + (j + 1) * QUARTERS)
                    act.activation(g_parts[:, j, 0, :], m_ps[j][:, :], ACT.Copy).then_inc(g_part1, 1)
                    act.wait_ge(dve_early, h * 2 + (A_STEPS + j + 1))
                    act.activation(g_parts[:, j, 1, :], g_rest[:, j, :], ACT.Copy).then_inc(g_part2, 1)
                    act.wait_ge(g_part2, h * 2 + (j + 1))
                    for k in range(2):
                        stacked = stack_g(h, j, k, lambda o, i: act.activation(o, i, ACT.Copy))
                    stacked.then_inc(act_stacked, 1)

            def copy_m(g, s, q):
                act.wait_ge(m_done, g * (SLOTS * QUARTERS) + (s * QUARTERS + q + 1))
                if s >= 2:
                    act.wait_ge(out_done, g * (SLOTS * CH) + (s - 1) * CH)
                act.activation(m_sb[s % 2][:, q * QW:(q + 1) * QW], m_ps[q % 2][:, :], ACT.Copy).then_inc(m_ready, 1)

            with act.Fori(0, ROUNDS) as g:
                for s in range(SLOTS):
                    act.wait_ge(bx_done, g * SLOTS + (s + 1))
                    if s >= 1:
                        act.wait_ge(hold_done, g * SLOTS + s)
                    act.activation(bx_sb[:, :], bx_ps[:, :], ACT.Copy).then_inc(bx_ready, 1)
                    act.wait_ge(shifted, g * SLOTS + (s + 1))
                    act.activation(e_b[:, :, :], e_a[:, :, :], ACT.Exp).then_inc(exp_ready, 1)
                    for q in range(QUARTERS):
                        copy_m(g, s, q)
                    act.wait_ge(zt_done, g * SLOTS + (s + 1))
                    act.activation(zt_sb[:, s % 2, :], bx_ps[:, :], ACT.Copy).then_inc(zt_ready, 1)
                act.wait_ge(out_done, g * (SLOTS * CH) + SLOTS * CH)

        @block.vector
        def _(dve):
            dve.wait_ge(a_loaded, 16 * BATCH)
            for c0 in (0, 2 * QC):
                pack_a(c0, dve.tensor_copy).then_inc(dve_early, 1)
            dve.wait_ge(ident_loaded, 16)
            dve.tensor_copy(own_sb, ident_sb[:, :].rearrange("p (b r) -> p b r", b=BATCH).unsqueeze(2).to_broadcast(
                [P, BATCH, P // RANK, RANK])).then_inc(own_ready, 1)
            with dve.Fori(0, QUARTERS // 2) as h:
                for j in range(2):
                    dve.wait_ge(g_part1, h * 2 + (j + 1))
                    dve.tensor_tensor(g_rest[:, j, :], m_ps[j][:, :], g_parts[:, j, 0, :], ALU.subtract).then_inc(dve_early, 1)
                    dve.wait_ge(g_part2, h * 2 + (j + 1))
                    dve.tensor_tensor(g_parts[:, j, 2, :], g_rest[:, j, :], g_parts[:, j, 1, :], ALU.subtract).then_inc(g_part3, 1)
                    dve.wait_ge(g_part3, h * 2 + (j + 1))
                    stack_g(h, j, 2, dve.tensor_copy).then_inc(dve_stacked, 1)
            dve.wait_ge(lg_done, 1)
            dve.tensor_scalar(lg_sb[:, RANK:HOLD], tok_ps[:, 0:EXPERTS], 0.5, None, ALU.mult).then_inc(dve_early, 1)
            dve.wait_ge(h_done, 1)
            dve.tensor_copy(h_sb[:, :, :].rearrange("p b r -> p (b r)"), bx_ps[:, 0:P]).then_inc(dve_early, 1)
            dve.wait_ge(head_done, 1)
            dve.tensor_copy(head_sb[:, :, :], head_ps).then_inc(dve_early, 1)

            def wide(c):
                return col[:, c, :].unsqueeze(2).to_broadcast([P, SUB, EXPERTS])

            N_STEPS = 20

            def routing(g, s):
                count = [0]

                def then(ins):
                    count[0] += 1
                    ins.then_inc(step, 1)
                    dve.wait_ge(step, g * (SLOTS * N_STEPS) + (s * N_STEPS + count[0]))

                dve.wait_ge(hold_done, g * SLOTS + (s + 1))
                then(dve.tensor_copy(hold_sb[:, :, :], hold_ps))
                logits = hold_sb[:, :, RANK:HOLD]
                then(dve.tensor_reduce(col[:, 0, :], logits, AX_X, ALU.max))
                dve.tensor_tensor(e_a[:, :, :], logits, wide(0), ALU.subtract).then_inc(shifted, 1)
                dve.wait_ge(exp_ready, g * SLOTS + (s + 1))
                then(dve.tensor_reduce(col[:, 1, :], e_b[:, :, :], AX_X, ALU.add))
                then(dve.reciprocal(col[:, 2, :], col[:, 1, :]))
                then(dve.tensor_tensor(e_a[:, :, :], e_b[:, :, :], wide(2), ALU.mult))
                then(dve.tensor_reduce(col[:, 3, :], e_a[:, :, :], AX_X, ALU.max))
                then(dve.tensor_tensor(e_b[:, :, :], e_a[:, :, :], wide(3), ALU.is_equal))
                then(dve.tensor_tensor(e_c[:, :, :], e_b[:, :, :], desc_sb[:, :, :], ALU.mult))
                then(dve.tensor_reduce(col[:, 4, :], e_c[:, :, :], AX_X, ALU.max))
                then(dve.tensor_tensor(e_b[:, :, :], e_c[:, :, :], wide(4), ALU.is_equal))
                then(dve.scalar_tensor_tensor(out=e_c[:, :, :], in0=e_b[:, :, :], scalar=-2.0, in1=e_a[:, :, :],
                                              op0=ALU.mult, op1=ALU.add))
                then(dve.tensor_reduce(col[:, 5, :], e_c[:, :, :], AX_X, ALU.max))
                then(dve.tensor_tensor(e_d[:, :, :], e_c[:, :, :], wide(5), ALU.is_equal))
                then(dve.tensor_tensor(e_c[:, :, :], e_d[:, :, :], desc_sb[:, :, :], ALU.mult))
                then(dve.tensor_reduce(col[:, 6, :], e_c[:, :, :], AX_X, ALU.max))
                then(dve.tensor_tensor(e_d[:, :, :], e_c[:, :, :], wide(6), ALU.is_equal))
                then(dve.tensor_tensor(e_c[:, :, :], e_b[:, :, :], e_d[:, :, :], ALU.add))
                then(dve.tensor_tensor(e_d[:, :, :], e_a[:, :, :], e_c[:, :, :], ALU.mult))
                then(dve.tensor_reduce(col[:, 7, :], e_d[:, :, :], AX_X, ALU.add))
                then(dve.reciprocal(col[:, 0, :], col[:, 7, :]))
                assert count[0] == N_STEPS
                dve.tensor_tensor(e_a[:, :, :], e_d[:, :, :], wide(0), ALU.mult).then_inc(route_ready, 1)
                dve.wait_ge(route_ready, g * SLOTS + (s + 1))
                if s >= 1:
                    dve.wait_ge(zt_done, g * SLOTS + s)
                for t in range(SUB):
                    z = dve.tensor_tensor(z_sb[:, t, :, :],
                                          hold_sb[:, t, 0:RANK].unsqueeze(1).to_broadcast([P, EXPERTS, RANK]),
                                          e_a[:, t, :].unsqueeze(2).to_broadcast([P, EXPERTS, RANK]), ALU.mult)
                z.then_inc(z_ready, 1)

            def diagonal(g, s):
                if s >= 2:
                    dve.wait_ge(m_done, g * (SLOTS * QUARTERS) + (s - 1) * QUARTERS)
                dve.tensor_tensor(hd_sb[:, s % 2, :, :], h_sb[:, bass.ds(g + 2 * s, 1), :].to_broadcast([P, EXPERTS, RANK]),
                                  block8_sb[:, :, :], ALU.mult).then_inc(hd_ready, 1)

            def finish(g, s, chunks):
                for c in chunks:
                    dve.wait_ge(out_done, g * (SLOTS * CH) + (s * CH + c + 1))
                    dve.scalar_tensor_tensor(out=x_sb[:, s, c, :], in0=out_ps[c % OUT_BANKS][:, :],
                                             scalar=bias_sb[:, c:c + 1], in1=x_sb[:, s, c, :],
                                             op0=ALU.add, op1=ALU.add).then_inc(out_ready, 1)

            dve.wait_ge(dve_early, G_STEPS + 3)
            dve.wait_ge(consts_loaded, 16 * N_CONSTS)
            with dve.Fori(0, ROUNDS) as g:
                dve.tensor_copy(fold_cur[:, :], fold_sb[:, bass.ds(g, 1), :].rearrange("p a k -> p (a k)")).then_inc(fold_ready, 1)
                diagonal(g, 0)
                routing(g, 0)
                for s in range(SLOTS):
                    last = s == SLOTS - 1
                    if not last:
                        diagonal(g, s + 1)
                    finish(g, s, range(0, 8))
                    if not last:
                        routing(g, s + 1)
                    finish(g, s, range(8, CH))

        @block.tensor
        def _(pe):
            with pe.Fori(0, QUARTERS // 2) as h:
                for j in range(2):
                    pe.wait_ge(dve_early, h * 2 + (j + A_STEPS - 1))
                    for s in range(QUARTERS):
                        pe.wait_ge(a_packed if s % 2 else dve_early, s // 2 + 1)
                        pe.wait_ge(w_loaded[s], h * 32 + 16 * (j + 1))
                        for i in range(QC):
                            c = s * QC + i
                            mm = pe.matmul(m_ps[j][:, :], a_cols[:, c, :], w_ring[:, s, i, :],
                                           start=(c == 0), stop=(c == CH - 1))
                        mm.then_inc(w_used, 1)
            pe.wait_ge(consts_loaded, 16 * N_CONSTS)
            for c in range(CH):
                mm = pe.matmul(tok_ps[:, 0:EXPERTS], a_cols[:, c, :], wg_sb[:, c, :], start=(c == 0), stop=(c == CH - 1))
            mm.then_inc(lg_done, 1)
            pe.wait_ge(ae_loaded, 16)
            for c in range(CH):
                mm = pe.matmul(bx_ps[:, 0:P], aeT_sb[:, c, :], a_cols[:, c, :], start=(c == 0), stop=(c == CH - 1))
            mm.then_inc(h_done, 1)
            pe.wait_ge(own_ready, 1)
            pe.wait_ge(dve_early, G_STEPS + 1)
            for b in range(BATCH):
                own = own_sb[:, b, :, :].rearrange("p k r -> p (k r)")
                mm = pe.matmul(head_ps[:, b, :], own, lg_sb[:, :], start=True, stop=True)
            mm.then_inc(head_done, 1)

            def multiply_b(g, s):
                pe.wait_ge(x_loaded[s], g * (16 * QUARTERS) + 16 * QUARTERS)
                pe.wait_ge(b_ready, g * SLOTS + (s + 1))
                if s >= 1:
                    pe.wait_ge(zt_ready, g * SLOTS + s)
                for c in range(CH):
                    j = c % STRIPS
                    own = b_sb[:, s, c, :, :].rearrange("p k r -> p (k r)")
                    mm = pe.matmul(bx_ps[32 * j:32 * (j + 1), :], own, x_sb[:, s, c, :],
                                   start=(c < STRIPS), stop=(c >= CH - STRIPS))
                mm.then_inc(bx_done, 1)

            def multiply_head(g, s):
                pe.wait_ge(bx_ready, g * SLOTS + (s + 1))
                if s >= 1:
                    pe.wait_ge(z_ready, g * SLOTS + s)
                for t in range(SUB):
                    mm = pe.matmul(hold_ps[:, t, :], bx_sb[:, t * P:(t + 1) * P],
                                   head_sb[:, bass.ds(g + 2 * s, 1), :].rearrange("p a h -> p (a h)"),
                                   start=True, stop=True)
                mm.then_inc(hold_done, 1)

            def multiply_m(g, s, quarters):
                for q in quarters:
                    if q == 0:
                        pe.wait_ge(hd_ready, g * SLOTS + (s + 1))
                    if s * QUARTERS + q >= 2:
                        pe.wait_ge(m_ready, g * (SLOTS * QUARTERS) + (s * QUARTERS + q - 1))
                    part = slice(q * QW, (q + 1) * QW)
                    pe.matmul(m_ps[q % 2][:, :], hd_sb[:, s % 2, :, :].rearrange("p e r -> p (e r)"), be_sb[:, part],
                              start=True, stop=False)
                    pe.matmul(m_ps[q % 2][:, :], fold_cur[:, :], g_stack[:, s, part],
                              start=False, stop=True).then_inc(m_done, 1)

            def turn_z(g, s):
                pe.wait_ge(z_ready, g * SLOTS + (s + 1))
                for t in range(SUB):
                    mm = pe.transpose(bx_ps[:, t * P:(t + 1) * P], z_sb[:, t, :, :].rearrange("p e r -> p (e r)"),
                                      ident_sb[:, :])
                mm.then_inc(zt_done, 1)

            def multiply_out(g, s, chunks):
                for c in chunks:
                    if c == 0:
                        pe.wait_ge(zt_ready, g * SLOTS + (s + 1))
                    if c % QC == 0:
                        pe.wait_ge(m_ready, g * (SLOTS * QUARTERS) + (s * QUARTERS + c // QC + 1))
                    if s * CH + c >= OUT_BANKS:
                        pe.wait_ge(out_ready, g * (SLOTS * CH) + (s * CH + c + 1 - OUT_BANKS))
                    pe.matmul(out_ps[c % OUT_BANKS][:, :], m_sb[s % 2][:, c * P:(c + 1) * P], zt_sb[:, s % 2, :],
                              start=True, stop=True).then_inc(out_done, 1)

            pe.wait_ge(be_loaded, 16)
            pe.wait_ge(act_stacked, QUARTERS)
            pe.wait_ge(dve_stacked, QUARTERS)
            pe.wait_ge(dve_early, G_STEPS + 3)
            with pe.Fori(0, ROUNDS) as g:
                multiply_b(g, 0)
                multiply_head(g, 0)
                pe.wait_ge(fold_ready, g + 1)
                multiply_m(g, 0, range(QUARTERS))
                turn_z(g, 0)
                for s in range(SLOTS):
                    nxt = s + 1 < SLOTS
                    multiply_out(g, s, range(0, 4))
                    if nxt:
                        multiply_b(g, s + 1)
                    multiply_out(g, s, range(4, 8))
                    if nxt:
                        multiply_head(g, s + 1)
                        multiply_m(g, s + 1, range(0, 2))
                    multiply_out(g, s, range(8, 12))
                    if nxt:
                        multiply_m(g, s + 1, range(2, 4))
                        turn_z(g, s + 1)
                    multiply_out(g, s, range(12, 16))
                pe.wait_ge(out_ready, g * (SLOTS * CH) + SLOTS * CH)


def kernel(x, itok_B_4_50, L0_cond_A, L0_cond_B, L0_ffn_W_base, L0_ffn_b_base, L0_ffn_W_gate, L0_ffn_A, L0_ffn_B):
    import ml_dtypes
    import numpy as np
    import concourse.bacc as bacc
    from concourse.bass_utils import run_bass_kernel_spmd

    def lay(a):
        return np.ascontiguousarray(a)

    x, W = np.asarray(x), np.asarray(L0_ffn_W_base)
    eye, rank_eye = np.eye(P, dtype=np.float32), np.eye(RANK, dtype=np.float32)
    arrays = {
        "xT": lay(x.reshape(BATCH, TOK, QUARTERS, QC, P).transpose(0, 2, 4, 3, 1)),
        "ids": lay(np.asarray(itok_B_4_50).reshape(1, BATCH)),
        "A": lay(np.asarray(L0_cond_A).reshape(-1, P, CH, RANK)),
        "B": lay(np.asarray(L0_cond_B).reshape(-1, RANK, CH, P).transpose(0, 3, 2, 1)),
        "WT": lay(W.reshape(QUARTERS, QW, P, QUARTERS, QC).transpose(0, 3, 2, 4, 1)),
        "bias": lay(np.asarray(L0_ffn_b_base).reshape(CH, P).T),
        "WgT": lay(np.asarray(L0_ffn_W_gate).reshape(EXPERTS, P, CH).transpose(1, 2, 0)),
        "AeT": lay(np.asarray(L0_ffn_A).reshape(EXPERTS * RANK, P, CH).transpose(1, 2, 0)),
        "BeT": lay(np.asarray(L0_ffn_B).transpose(0, 2, 1).reshape(EXPERTS * RANK, DIM)),
        "fold": lay(np.tile(np.eye(QUAD, dtype=np.float32).reshape(QUAD, ROUNDS, 1, RANK), (PARTS, 1, EXPERTS, 1)).reshape(
            PARTS * QUAD, ROUNDS, P).astype(ml_dtypes.bfloat16)),
        "spread": lay(np.tile(rank_eye * 0.5, (BATCH, 1))),
        "block8": lay(np.kron(np.eye(EXPERTS, dtype=np.float32), np.ones((RANK, RANK), np.float32)).reshape(P, EXPERTS, RANK)),
        "rank_desc": lay(np.broadcast_to(np.arange(EXPERTS, 0, -1, dtype=np.float32), (P, SUB, EXPERTS))),
        "ident": eye,
    }
    nc = bacc.Bacc("TRN2", target_bir_lowering=False, num_devices=1)
    args = [nc.dram_tensor(name, a.shape, mybir.dt.from_np(a.dtype), kind="ExternalInput").ap()
            for name, a in arrays.items()]
    out = nc.dram_tensor("out", (BATCH, QUARTERS, P, QC, TOK), F32, kind="ExternalOutput").ap()
    adaln_ffn_kernel(nc, *args, out)
    r = run_bass_kernel_spmd(nc, [arrays], core_ids=[0])
    got = r.results[0]["out"].reshape(BATCH, QUARTERS, P, QC, TOK)
    return lay(got.transpose(0, 4, 1, 3, 2).reshape(BATCH, TOK, DIM))
```

```python
from contextlib import ExitStack, nullcontext
from functools import partial

import concourse.bass as bass
from concourse import mybir

F32 = mybir.dt.float32
BF16 = mybir.dt.bfloat16
I32 = mybir.dt.int32
ALU = mybir.AluOpType
ACT = mybir.ActivationFunctionType
AX_X = mybir.AxisListType.X

P = 128
BATCH, TOK, DIM = 8, 512, 2048
RANK = 16
EXPERTS = 8
CH = DIM // P
QUARTERS = 4
QW = DIM // QUARTERS
QC = CH // QUARTERS
SLOTS = 4
ROUNDS = BATCH // SLOTS
STRIPS = 4
SUB = TOK // P
OUT_BANKS = 4
PARTS = 3
HOLD = RANK + EXPERTS
EG = EXPERTS * RANK + EXPERTS
QUAD = P // 4
SP_GATHERS, ACT_GATHERS = (0, 2, 4, 6, 7), (1, 3, 5)
WARM_UP = 5
A_STEPS = 2
G_STEPS = A_STEPS + QUARTERS
LT_STEP, HT_STEP, H_STEP, HEAD_STEP = (G_STEPS + n for n in range(1, 5))



def place(b):
    return 2 * (b % SLOTS) + b // SLOTS


def adaln_ffn_kernel(nc, xT, ids, A, B, WT, bias, EgT, BeT, fold, spread, block8, rank_desc, ident, out):
    with ExitStack() as ctx:
        def sb(name, shape, dt):
            return ctx.enter_context(nc.sbuf_tensor(name, shape, dt))

        def ps(name, shape):
            return ctx.enter_context(nc.psum_tensor(name, shape, F32))

        def sem(name):
            return ctx.enter_context(nc.semaphore(name))

        x_sb = sb("x_sb", [P, SLOTS, CH, TOK], F32)
        w_ring = x_sb[:, SLOTS - 1, :, :].rearrange("p (s c) n -> p s c n", s=QUARTERS)
        early = x_sb[:, SLOTS - 2, :, :].rearrange("p c n -> p (c n)")
        a_raw = early[:, 0:DIM].rearrange("p (b c r) -> p b c r", b=BATCH, c=CH)
        own_sb = early[:, DIM:DIM + BATCH * P].rearrange("p (b k r) -> p b k r", b=BATCH, r=RANK)
        ht_sb = early[:, DIM + BATCH * P:DIM + (BATCH + 1) * P]
        eg_sb = early[:, 2 * DIM:2 * DIM + CH * EG].rearrange("p (c n) -> p c n", c=CH)
        a_m1 = sb("a_m1", [P, DIM], F32)
        a_sb = a_m1[:, :].rearrange("p (c b r) -> p c b r", c=CH, b=BATCH)
        a_cols = a_m1[:, :].rearrange("p (c k) -> p c k", c=CH)
        m0_sb = sb("m0_sb", [P, DIM], F32)
        m_sb = [m0_sb, a_m1]
        b_raw = sb("b_raw", [P, SLOTS, CH, RANK], F32)
        b_sb = sb("b_sb", [P, SLOTS, CH, 2, RANK], F32)
        be_sb = sb("be_sb", [P, DIM], F32)
        bias_sb = sb("bias_sb", [P, CH], F32)
        ids_sb = sb("ids_sb", [1, BATCH], I32)
        g_parts = sb("g_parts", [P, 2, PARTS, QW], BF16)
        g_rest = sb("g_rest", [P, 2, QW], F32)
        g_stack = sb("g_stack", [PARTS * QUAD, SLOTS, DIM], BF16)
        lg_sb = sb("lg_sb", [P, HOLD], F32)
        head_sb = sb("head_sb", [P, BATCH, HOLD], F32)
        h_sb = sb("h_sb", [P, BATCH, RANK], F32)
        hd_sb = sb("hd_sb", [P, 2, EXPERTS, RANK], F32)
        fold_sb = sb("fold_sb", [PARTS * QUAD, ROUNDS, P], BF16)
        fold_cur = sb("fold_cur", [PARTS * QUAD, 2, P], BF16)
        block8_sb = sb("block8_sb", [P, EXPERTS, RANK], F32)
        desc_sb = sb("desc_sb", [P, SUB, EXPERTS], F32)
        ident_sb = sb("ident_sb", [P, P], F32)
        bx_sb = sb("bx_sb", [P, TOK], F32)
        z_sb = sb("z_sb", [P, SUB, EXPERTS, RANK], F32)
        zt_sb = sb("zt_sb", [P, 2, TOK], F32)
        e_a = sb("e_a", [P, SUB, EXPERTS], F32)
        e_b = sb("e_b", [P, SUB, EXPERTS], F32)
        e_c = sb("e_c", [P, SUB, EXPERTS], F32)
        e_d = sb("e_d", [P, SUB, EXPERTS], F32)
        col = sb("col", [P, 8, SUB], F32)

        out_ps = [ps(f"out_ps{i}", [P, TOK]) for i in range(OUT_BANKS)]
        m_ps = [ps(f"m_ps{i}", [P, QW]) for i in range(2)]
        bx_ps = ps("bx_ps", [P, TOK])
        tok_ps = ps("tok_ps", [P, TOK])
        hl_ps = tok_ps[:, 0:EG]
        hold_ps = tok_ps[:, 0:SUB * HOLD].rearrange("p (s h) -> p s h", s=SUB)
        head_ps = tok_ps[:, 0:BATCH * HOLD].rearrange("p (b h) -> p b h", b=BATCH)

        ids_loaded = sem("ids_loaded")
        a_loaded = sem("a_loaded")
        be_loaded = sem("be_loaded")
        eg_loaded = sem("eg_loaded")
        consts_loaded = sem("consts_loaded")
        ident_loaded = sem("ident_loaded")
        b_loaded = [sem(f"b_loaded{i}") for i in range(SLOTS)]
        a_packed = sem("a_packed")
        own_ready = sem("own_ready")
        b_ready = sem("b_ready")
        w_loaded = [sem(f"w_loaded{i}") for i in range(QUARTERS)]
        w_used = sem("w_used")
        x_loaded = [sem(f"x_loaded{i}") for i in range(SLOTS)]
        x_stored = [sem(f"x_stored{i}") for i in range(SLOTS)]
        hl_done = sem("hl_done")
        h_turned = sem("h_turned")
        head_done = sem("head_done")
        dve_early = sem("dve_early")
        g_part1 = sem("g_part1")
        g_part2 = sem("g_part2")
        g_part3 = sem("g_part3")
        act_stacked = sem("act_stacked")
        dve_stacked = sem("dve_stacked")
        hd_ready = sem("hd_ready")
        bx_done = sem("bx_done")
        bx_ready = sem("bx_ready")
        hold_done = sem("hold_done")
        step = sem("step")
        shifted = sem("shifted")
        exp_ready = sem("exp_ready")
        z_ready = sem("z_ready")
        zt_done = sem("zt_done")
        zt_ready = sem("zt_ready")
        m_done = sem("m_done")
        m_ready = sem("m_ready")
        out_done = sem("out_done")
        out_ready = sem("out_ready")

        N_CONSTS = 5
        block = ctx.enter_context(nc.Block())

        def gather_a(eng, b, index):
            p = place(b)
            eng.dma_start(a_raw[:, p:p + 1, :, :], A[bass.ds(index, 1)].rearrange("a p c r -> p a c r")).then_inc(a_loaded, 16)

        def pack_a(c0, copy):
            return copy(a_sb[:, c0:c0 + QC, :, :], a_raw[:, :, c0:c0 + QC, :].rearrange("p b c r -> p c b r"))

        def stack_g(h, j, k, copy):
            for s in range(SLOTS):
                last = copy(g_stack[k * QUAD:(k + 1) * QUAD, s, bass.ds(h * (2 * QW) + j * QW, QW)],
                            g_parts[s * QUAD:(s + 1) * QUAD, j, k, :])
            return last

        @block.sync
        def _(sp):
            sp.dma_start(ids_sb[:, :], ids).then_inc(ids_loaded, 16)

            def load_w(q, s):
                sp.dma_start(w_ring[:, s, :, :], WT[q, s]).then_inc(w_loaded[s], 16)

            load_w(0, 0)
            sp.wait_ge(ids_loaded, 16)
            which = [None] * BATCH
            for b in SP_GATHERS:
                which[b] = sp.value_load(ids_sb[0:1, b:b + 1], min_val=0, max_val=A.shape[0] - 1)
                gather_a(sp, b, which[b])
            for s in range(1, QUARTERS):
                load_w(0, s)
            for b in ACT_GATHERS:
                which[b] = sp.value_load(ids_sb[0:1, b:b + 1], min_val=0, max_val=B.shape[0] - 1)

            def load_b(b, s):
                sp.dma_start(b_raw[:, s:s + 1, :, :], B[bass.ds(which[b], 1)].rearrange("a p c r -> p a c r")).then_inc(b_loaded[s], 16)

            def load_x(b, s, quarters=range(QUARTERS)):
                for q in quarters:
                    sp.dma_start(x_sb[:, s, q * QC:(q + 1) * QC, :], xT[b, q]).then_inc(x_loaded[s], 16)

            load_b(0, 0)
            with sp.Fori(1, QUARTERS - 1) as q:
                for s in range(QUARTERS):
                    sp.wait_ge(w_used, q * QUARTERS + (s + 1 - QUARTERS))
                    sp.dma_start(w_ring[:, s, :, :], WT[bass.ds(q, 1), s].rearrange("a p c n -> p (a c) n")).then_inc(w_loaded[s], 16)
                sp.dma_start(x_sb[:, 0, bass.ds(q * QC - QC, QC), :],
                             xT[0, bass.ds(q - 1, 1)].rearrange("a p c n -> p (a c) n")).then_inc(x_loaded[0], 16)
            for s in range(QUARTERS):
                sp.wait_ge(w_used, (QUARTERS - 2) * QUARTERS + s + 1)
                load_w(QUARTERS - 1, s)
            sp.dma_start(eg_sb, EgT).then_inc(eg_loaded, 16)
            load_x(0, 0, range(QUARTERS - 2, QUARTERS))
            sp.dma_start(be_sb[:, :], BeT).then_inc(be_loaded, 16)
            load_b(1, 1)
            load_x(1, 1)
            sp.wait_ge(w_used, QUARTERS * QUARTERS)
            sp.wait_ge(head_done, 1)
            for s in range(2, SLOTS):
                load_b(s, s)
                load_x(s, s)

            def store(b, s, pieces=(QC,) * QUARTERS):
                c = 0
                for n in pieces:
                    sp.wait_ge(out_ready, OUT_BANKS + b * CH + c + n)
                    sp.dma_start(out[b, c // QC, :, c % QC:c % QC + n, :], x_sb[:, s, c:c + n, :]).then_inc(x_stored[s], 16)
                    c += n

            for s in range(SLOTS):
                store(s, s)
                if s > 0:
                    sp.wait_ge(x_stored[s - 1], 16 * QUARTERS)
                    load_b(SLOTS + s - 1, s - 1)
                    load_x(SLOTS + s - 1, s - 1)
            sp.wait_ge(x_stored[SLOTS - 1], 16 * QUARTERS)
            load_b(BATCH - 1, SLOTS - 1)
            load_x(BATCH - 1, SLOTS - 1)
            for s in range(SLOTS - 2):
                store(SLOTS + s, s)
            small = (QC // 2,) * (2 * QUARTERS)
            smallest = small[:-1] + (1,) * (QC // 2)
            store(BATCH - 2, SLOTS - 2, small)
            store(BATCH - 1, SLOTS - 1, smallest)
            for s in range(SLOTS - 2):
                sp.wait_ge(x_stored[s], ROUNDS * 16 * QUARTERS)
            sp.wait_ge(x_stored[SLOTS - 2], 16 * (QUARTERS + len(small)))
            sp.wait_ge(x_stored[SLOTS - 1], 16 * (QUARTERS + len(smallest)))

        @block.gpsimd
        def _(pool):
            def double_b(b):
                pool.wait_ge(b_loaded[b % SLOTS], 16 * (b // SLOTS + 1))
                if b >= SLOTS:
                    pool.wait_ge(bx_done, b - SLOTS + 1)
                pool.tensor_copy(b_sb[:, b % SLOTS, :, :, :],
                                 b_raw[:, b % SLOTS, :, :].unsqueeze(2).to_broadcast([P, CH, 2, RANK])).then_inc(b_ready, 1)

            for b in range(BATCH):
                double_b(b)

        @block.scalar
        def _(act):
            act.wait_ge(ids_loaded, 16)
            for b in ACT_GATHERS:
                gather_a(act, b, act.value_load(ids_sb[0:1, b:b + 1], min_val=0, max_val=A.shape[0] - 1))
            act.dma_start(ident_sb[:, :], ident).then_inc(ident_loaded, 16)
            act.dma_start(bias_sb[:, :], bias).then_inc(consts_loaded, 16)
            act.dma_start(fold_sb[:, :, :], fold).then_inc(consts_loaded, 16)
            act.dma_start(block8_sb[:, :, :], block8).then_inc(consts_loaded, 16)
            act.dma_start(desc_sb[:, :, :], rank_desc).then_inc(consts_loaded, 16)
            act.dma_start(lg_sb[:, 0:RANK], spread).then_inc(consts_loaded, 16)
            act.wait_ge(a_loaded, 16 * BATCH)
            for c0 in (QC, 3 * QC):
                pack_a(c0, lambda o, i: act.activation(o, i, ACT.Copy)).then_inc(a_packed, 1)

            with act.Fori(0, QUARTERS // 2) as h:
                for j in range(2):
                    act.wait_ge(w_used, h * (2 * QUARTERS) + (j + 1) * QUARTERS)
                    act.activation(g_parts[:, j, 0, :], m_ps[j][:, :], ACT.Copy).then_inc(g_part1, 1)
                    act.wait_ge(dve_early, h * 2 + (A_STEPS + j + 1))
                    act.activation(g_parts[:, j, 1, :], g_rest[:, j, :], ACT.Copy).then_inc(g_part2, 1)
                    act.wait_ge(g_part2, h * 2 + (j + 1))
                    for k in range(2):
                        stacked = stack_g(h, j, k, lambda o, i: act.activation(o, i, ACT.Copy))
                    stacked.then_inc(act_stacked, 1)

            def copy_m(g, s, q):
                act.wait_ge(m_done, g * (SLOTS * QUARTERS) + (s * QUARTERS + q + 1))
                act.activation(m_sb[s % 2][:, q * QW:(q + 1) * QW], m_ps[q % 2][:, :], ACT.Copy).then_inc(m_ready, 1)

            with act.Fori(0, ROUNDS) as g:
                for s in range(SLOTS):
                    act.wait_ge(bx_done, g * SLOTS + (s + 1))
                    if s >= 1:
                        act.wait_ge(hold_done, g * SLOTS + s)
                    act.activation(bx_sb[:, :], bx_ps[:, :], ACT.Copy).then_inc(bx_ready, 1)
                    act.wait_ge(shifted, g * SLOTS + (s + 1))
                    act.activation(e_b[:, :, :], e_a[:, :, :], ACT.Exp).then_inc(exp_ready, 1)
                    for q in range(QUARTERS):
                        copy_m(g, s, q)
                    act.wait_ge(zt_done, g * SLOTS + (s + 1))
                    act.activation(zt_sb[:, s % 2, :], bx_ps[:, :], ACT.Copy).then_inc(zt_ready, 1)

        @block.vector
        def _(dve):
            for t in range(OUT_BANKS):
                dve.memset(z_sb[:, t, :, :], 0.0).then_inc(out_ready, 1)
            dve.wait_ge(a_loaded, 16 * BATCH)
            for c0 in (0, 2 * QC):
                pack_a(c0, dve.tensor_copy).then_inc(dve_early, 1)
            dve.wait_ge(ident_loaded, 16)
            dve.tensor_copy(own_sb, ident_sb[:, :].rearrange("p (b r) -> p b r", b=BATCH).unsqueeze(2).to_broadcast(
                [P, BATCH, P // RANK, RANK])).then_inc(own_ready, 1)
            with dve.Fori(0, QUARTERS // 2) as h:
                for j in range(2):
                    dve.wait_ge(g_part1, h * 2 + (j + 1))
                    dve.tensor_tensor(g_rest[:, j, :], m_ps[j][:, :], g_parts[:, j, 0, :], ALU.subtract).then_inc(dve_early, 1)
                    dve.wait_ge(g_part2, h * 2 + (j + 1))
                    dve.tensor_tensor(g_parts[:, j, 2, :], g_rest[:, j, :], g_parts[:, j, 1, :], ALU.subtract).then_inc(g_part3, 1)
                    dve.wait_ge(g_part3, h * 2 + (j + 1))
                    stack_g(h, j, 2, dve.tensor_copy).then_inc(dve_stacked, 1)
            dve.wait_ge(consts_loaded, 16 * N_CONSTS)
            dve.wait_ge(hl_done, 1)
            dve.tensor_scalar(lg_sb[:, RANK:HOLD], hl_ps[:, EG - EXPERTS:EG], 0.5, None, ALU.mult).then_inc(dve_early, 1)
            dve.tensor_copy(ht_sb, hl_ps[:, 0:P]).then_inc(dve_early, 1)
            dve.wait_ge(h_turned, 1)
            dve.tensor_copy(h_sb[:, :, :].rearrange("p b r -> p (b r)"), out_ps[0][:, 0:P]).then_inc(dve_early, 1)
            dve.wait_ge(head_done, 1)
            dve.tensor_copy(head_sb[:, :, :], head_ps).then_inc(dve_early, 1)

            def wide(c):
                return col[:, c, :].unsqueeze(2).to_broadcast([P, SUB, EXPERTS])

            N_STEPS = 18

            def routing(g, s):
                count = [0]

                def then(ins):
                    count[0] += 1
                    ins.then_inc(step, 1)
                    dve.wait_ge(step, g * (SLOTS * N_STEPS) + (s * N_STEPS + count[0]))

                dve.wait_ge(hold_done, g * SLOTS + (s + 1))
                logits = hold_ps[:, :, RANK:HOLD]
                then(dve.tensor_reduce(col[:, 0, :], logits, AX_X, ALU.max))
                dve.tensor_tensor(e_a[:, :, :], logits, wide(0), ALU.subtract).then_inc(shifted, 1)
                dve.wait_ge(exp_ready, g * SLOTS + (s + 1))
                then(dve.tensor_reduce(col[:, 1, :], e_b[:, :, :], AX_X, ALU.add))
                then(dve.reciprocal(col[:, 6, :], col[:, 1, :]))
                then(dve.tensor_tensor(e_a[:, :, :], e_b[:, :, :], wide(6), ALU.mult))
                then(dve.tensor_reduce(col[:, 2, :], e_a[:, :, :], AX_X, ALU.max))
                then(dve.tensor_tensor(e_b[:, :, :], e_a[:, :, :], wide(2), ALU.is_equal))
                then(dve.tensor_tensor(e_c[:, :, :], e_b[:, :, :], desc_sb[:, :, :], ALU.mult))
                then(dve.tensor_reduce(col[:, 3, :], e_c[:, :, :], AX_X, ALU.max))
                then(dve.tensor_tensor(e_b[:, :, :], e_c[:, :, :], wide(3), ALU.is_equal))
                then(dve.scalar_tensor_tensor(out=e_c[:, :, :], in0=e_b[:, :, :], scalar=-2.0, in1=e_a[:, :, :],
                                              op0=ALU.mult, op1=ALU.add))
                then(dve.tensor_reduce(col[:, 4, :], e_c[:, :, :], AX_X, ALU.max))
                then(dve.tensor_tensor(e_d[:, :, :], e_c[:, :, :], wide(4), ALU.is_equal))
                then(dve.tensor_tensor(e_c[:, :, :], e_d[:, :, :], desc_sb[:, :, :], ALU.mult))
                then(dve.tensor_reduce(col[:, 5, :], e_c[:, :, :], AX_X, ALU.max))
                then(dve.tensor_tensor(e_d[:, :, :], e_c[:, :, :], wide(5), ALU.is_equal))
                dve.tensor_tensor(col[:, 6, :], col[:, 2, :], col[:, 4, :], ALU.add)
                then(dve.tensor_tensor(e_c[:, :, :], e_b[:, :, :], e_d[:, :, :], ALU.add))
                dve.reciprocal(col[:, 7, :], col[:, 6, :])
                then(dve.tensor_tensor(e_d[:, :, :], e_a[:, :, :], e_c[:, :, :], ALU.mult))
                then(dve.tensor_tensor(e_a[:, :, :], e_d[:, :, :], wide(7), ALU.mult))
                assert count[0] == N_STEPS
                if s >= 1:
                    dve.wait_ge(zt_done, g * SLOTS + s)
                for t in range(SUB):
                    dve.tensor_tensor(z_sb[:, t, :, :],
                                      hold_ps[:, t, 0:RANK].unsqueeze(1).to_broadcast([P, EXPERTS, RANK]),
                                      e_a[:, t, :].unsqueeze(2).to_broadcast([P, EXPERTS, RANK]), ALU.mult).then_inc(z_ready, 1)

            def diagonal(g, s):
                if s >= 2:
                    dve.wait_ge(m_done, g * (SLOTS * QUARTERS) + (s - 1) * QUARTERS)
                dve.tensor_tensor(hd_sb[:, s % 2, :, :], h_sb[:, bass.ds(g + place(s), 1), :].to_broadcast([P, EXPERTS, RANK]),
                                  block8_sb[:, :, :], ALU.mult).then_inc(hd_ready, 1)
                dve.tensor_copy(fold_cur[:, s % 2, :], fold_sb[:, bass.ds(g + s // SLOTS, 1), :].rearrange("p a k -> p (a k)")).then_inc(hd_ready, 1)

            def finish(g, s, chunks):
                for c in chunks:
                    dve.wait_ge(out_done, g * (SLOTS * CH) + (s * CH + c + 1))
                    dve.scalar_tensor_tensor(out=x_sb[:, s, c, :], in0=out_ps[c % OUT_BANKS][:, :],
                                             scalar=bias_sb[:, c:c + 1], in1=x_sb[:, s, c, :],
                                             op0=ALU.add, op1=ALU.add).then_inc(out_ready, 1)

            dve.wait_ge(dve_early, H_STEP)
            diagonal(0, 0)
            routing(0, 0)
            with dve.Fori(0, ROUNDS) as g:
                for s in range(SLOTS):
                    more = partial(dve.If, g < ROUNDS - 1) if s == SLOTS - 1 else nullcontext
                    gn = 0 if s == SLOTS - 1 else g
                    with more():
                        diagonal(gn, s + 1)
                    finish(g, s, range(0, 8))
                    with more():
                        routing(gn, s + 1)
                    finish(g, s, range(8, CH))

        @block.tensor
        def _(pe):
            pe.wait_ge(out_ready, OUT_BANKS)
            warm = z_sb[:, :, :, :].rearrange("p t e r -> p (t e r)")
            for n in range(WARM_UP):
                pe.matmul(out_ps[0][:, :], warm[:, 0:P], warm, start=True, stop=True)
            with pe.Fori(0, QUARTERS // 2) as h:
                for j in range(2):
                    pe.wait_ge(dve_early, h * 2 + (j + A_STEPS - 1))
                    for s in range(QUARTERS):
                        pe.wait_ge(a_packed if s % 2 else dve_early, s // 2 + 1)
                        pe.wait_ge(w_loaded[s], h * 32 + 16 * (j + 1))
                        for i in range(QC):
                            c = s * QC + i
                            mm = pe.matmul(m_ps[j][:, :], a_cols[:, c, :], w_ring[:, s, i, :],
                                           start=(c == 0), stop=(c == CH - 1))
                        mm.then_inc(w_used, 1)
            pe.wait_ge(eg_loaded, 16)
            for c in range(CH):
                mm = pe.matmul(hl_ps, a_cols[:, c, :], eg_sb[:, c, :], start=(c == 0), stop=(c == CH - 1))
            mm.then_inc(hl_done, 1)

            def multiply_b(g, s):
                slot = s % SLOTS
                pe.wait_ge(x_loaded[slot], g * (16 * QUARTERS) + 16 * QUARTERS * (s // SLOTS + 1))
                pe.wait_ge(b_ready, g * SLOTS + (s + 1))
                if s >= 1:
                    pe.wait_ge(zt_ready, g * SLOTS + s)
                for c in range(CH):
                    j = c % STRIPS
                    own = b_sb[:, slot, c, :, :].rearrange("p k r -> p (k r)")
                    mm = pe.matmul(bx_ps[32 * j:32 * (j + 1), :], own, x_sb[:, slot, c, :],
                                   start=(c < STRIPS), stop=(c >= CH - STRIPS))
                mm.then_inc(bx_done, 1)

            def multiply_head(g, s):
                pe.wait_ge(bx_ready, g * SLOTS + (s + 1))
                if s >= 1:
                    pe.wait_ge(z_ready, g * (SLOTS * SUB) + s * SUB)
                for t in range(SUB):
                    mm = pe.matmul(hold_ps[:, t, :], bx_sb[:, t * P:(t + 1) * P],
                                   head_sb[:, bass.ds(g + place(s), 1), :].rearrange("p a h -> p (a h)"),
                                   start=True, stop=True)
                mm.then_inc(hold_done, 1)

            def multiply_m(g, s, quarters):
                for q in quarters:
                    if q == 0:
                        pe.wait_ge(hd_ready, g * (2 * SLOTS) + 2 * (s + 1))
                    if s * QUARTERS + q >= 2:
                        pe.wait_ge(m_ready, g * (SLOTS * QUARTERS) + (s * QUARTERS + q - 1))
                    part = slice(q * QW, (q + 1) * QW)
                    pe.matmul(m_ps[q % 2][:, :], hd_sb[:, s % 2, :, :].rearrange("p e r -> p (e r)"), be_sb[:, part],
                              start=True, stop=False)
                    pe.matmul(m_ps[q % 2][:, :], fold_cur[:, s % 2, :], g_stack[:, s % SLOTS, part],
                              start=False, stop=True).then_inc(m_done, 1)

            def turn_z(g, s):
                for t in range(SUB):
                    pe.wait_ge(z_ready, g * (SLOTS * SUB) + (s * SUB + t + 1))
                    mm = pe.transpose(bx_ps[:, t * P:(t + 1) * P], z_sb[:, t, :, :].rearrange("p e r -> p (e r)"),
                                      ident_sb[:, :])
                mm.then_inc(zt_done, 1)

            def multiply_out(g, s, chunks):
                for c in chunks:
                    if c == 0:
                        pe.wait_ge(zt_ready, g * SLOTS + (s + 1))
                    if c % QC == 0:
                        pe.wait_ge(m_ready, g * (SLOTS * QUARTERS) + (s * QUARTERS + c // QC + 1))
                    pe.wait_ge(out_ready, g * (SLOTS * CH) + (s * CH + c + 1))
                    pe.matmul(out_ps[c % OUT_BANKS][:, :], m_sb[s % 2][:, c * P:(c + 1) * P], zt_sb[:, s % 2, :],
                              start=True, stop=True).then_inc(out_done, 1)

            multiply_b(0, 0)
            pe.wait_ge(dve_early, HT_STEP)
            pe.transpose(out_ps[0][:, 0:P], ht_sb, ident_sb[:, :]).then_inc(h_turned, 1)
            pe.wait_ge(own_ready, 1)
            for b in range(BATCH):
                own = own_sb[:, b, :, :].rearrange("p k r -> p (k r)")
                mm = pe.matmul(head_ps[:, b, :], own, lg_sb[:, :], start=True, stop=True)
            mm.then_inc(head_done, 1)
            pe.wait_ge(dve_early, HEAD_STEP)
            multiply_head(0, 0)
            pe.wait_ge(be_loaded, 16)
            pe.wait_ge(act_stacked, QUARTERS)
            pe.wait_ge(dve_stacked, QUARTERS)
            multiply_m(0, 0, range(QUARTERS))
            turn_z(0, 0)
            with pe.Fori(0, ROUNDS) as g:
                for s in range(SLOTS):
                    more = partial(pe.If, g < ROUNDS - 1) if s == SLOTS - 1 else nullcontext
                    gn = 0 if s == SLOTS - 1 else g
                    multiply_out(g, s, range(0, 4))
                    with more():
                        multiply_b(gn, s + 1)
                    multiply_out(g, s, range(4, 8))
                    with more():
                        multiply_head(gn, s + 1)
                        multiply_m(gn, s + 1, range(0, 2))
                    multiply_out(g, s, range(8, 12))
                    with more():
                        multiply_m(gn, s + 1, range(2, 4))
                        turn_z(gn, s + 1)
                    multiply_out(g, s, range(12, 16))


def kernel(x, itok_B_4_50, L0_cond_A, L0_cond_B, L0_ffn_W_base, L0_ffn_b_base, L0_ffn_W_gate, L0_ffn_A, L0_ffn_B):
    import ml_dtypes
    import numpy as np
    import concourse.bacc as bacc
    from concourse.bass_utils import run_bass_kernel_spmd

    def lay(a):
        return np.ascontiguousarray(a)

    x, W = np.asarray(x), np.asarray(L0_ffn_W_base)
    eye, rank_eye = np.eye(P, dtype=np.float32), np.eye(RANK, dtype=np.float32)
    arrays = {
        "xT": lay(x.reshape(BATCH, TOK, QUARTERS, QC, P).transpose(0, 2, 4, 3, 1)),
        "ids": lay(np.asarray(itok_B_4_50).reshape(1, BATCH)),
        "A": lay(np.asarray(L0_cond_A).reshape(-1, P, CH, RANK)),
        "B": lay(np.asarray(L0_cond_B).reshape(-1, RANK, CH, P).transpose(0, 3, 2, 1)),
        "WT": lay(W.reshape(QUARTERS, QW, P, QUARTERS, QC).transpose(0, 3, 2, 4, 1)),
        "bias": lay(np.asarray(L0_ffn_b_base).reshape(CH, P).T),
        "EgT": lay(np.concatenate([np.asarray(L0_ffn_A).reshape(EXPERTS * RANK, P, CH),
                                   np.asarray(L0_ffn_W_gate).reshape(EXPERTS, P, CH)]).transpose(1, 2, 0)),
        "BeT": lay(np.asarray(L0_ffn_B).transpose(0, 2, 1).reshape(EXPERTS * RANK, DIM)),
        "fold": lay(np.tile(np.eye(QUAD, dtype=np.float32).reshape(QUAD, ROUNDS, 1, RANK), (PARTS, 1, EXPERTS, 1)).reshape(
            PARTS * QUAD, ROUNDS, P).astype(ml_dtypes.bfloat16)),
        "spread": lay(np.tile(rank_eye * 0.5, (BATCH, 1))),
        "block8": lay(np.kron(np.eye(EXPERTS, dtype=np.float32), np.ones((RANK, RANK), np.float32)).reshape(P, EXPERTS, RANK)),
        "rank_desc": lay(np.broadcast_to(np.arange(EXPERTS, 0, -1, dtype=np.float32), (P, SUB, EXPERTS))),
        "ident": eye,
    }
    nc = bacc.Bacc("TRN2", target_bir_lowering=False, num_devices=1)
    args = [nc.dram_tensor(name, a.shape, mybir.dt.from_np(a.dtype), kind="ExternalInput").ap()
            for name, a in arrays.items()]
    out = nc.dram_tensor("out", (BATCH, QUARTERS, P, QC, TOK), F32, kind="ExternalOutput").ap()
    adaln_ffn_kernel(nc, *args, out)
    r = run_bass_kernel_spmd(nc, [arrays], core_ids=[0])
    got = r.results[0]["out"].reshape(BATCH, QUARTERS, P, QC, TOK)
    return lay(got.transpose(0, 4, 1, 3, 2).reshape(BATCH, TOK, DIM))
```
